# Optimizing a Trainium2 kernel written in Bass

```python
import numpy as np
import jax
import jax.numpy as jnp

def _softmax(x, axis=-1):
    return jax.nn.softmax(x, axis=axis)

def _gelu(x):
    return jax.nn.gelu(x, approximate=True)

def _silu(x):
    return jax.nn.silu(x)

def _sigmoid(x):
    return jax.nn.sigmoid(x)

def _layernorm(x, axis=-1, eps=1e-05):
    m = jnp.mean(x, axis=axis, keepdims=True)
    v = jnp.var(x, axis=axis, keepdims=True)
    return (x - m) / jnp.sqrt(v + eps)

def _scatter_add(tgt, idx, src, axis=0):
    return tgt.at[idx].add(src)

def _segment_sum(src, seg, n):
    return jax.ops.segment_sum(src, seg, n)
kernel_name = 'mk_dlrm_tower_d1_rec_r8_73150f'

def setup_inputs(seed: int=0):
    np.random.seed(seed)
    _w = jnp.asarray

    def _rec_inputs():
        import jax
        import jax.numpy as jnp
        _tk = jax.random.key(seed)
        dense_ctx = jax.random.normal(jax.random.fold_in(_tk, 190), (1024, 16), jnp.float32)
        ids = jnp.stack([jax.random.randint(jax.random.fold_in(_tk, 200 + f), (1024,), 0, v, jnp.int32) for f, v in enumerate([125000, 1000, 1250, 1000, 1000, 1000, 125000, 1000, 125000, 1250, 12500, 1000, 12500, 125000, 125000, 1250, 1000, 12500, 1250, 12500, 12500, 1000, 1000, 1250, 1000, 1000, 1000, 1000, 1000, 12500, 125000, 1000, 125000, 125000, 1000, 12500, 1250, 125000, 125000])], axis=1)
        tbl_0 = 0.05 * jax.random.normal(jax.random.fold_in(_tk, 500 + 0), (125000, 16), jnp.float32)
        tbl_1 = 0.05 * jax.random.normal(jax.random.fold_in(_tk, 500 + 1), (1000, 16), jnp.float32)
        tbl_2 = 0.05 * jax.random.normal(jax.random.fold_in(_tk, 500 + 2), (1250, 16), jnp.float32)
        tbl_3 = 0.05 * jax.random.normal(jax.random.fold_in(_tk, 500 + 3), (1000, 16), jnp.float32)
        tbl_4 = 0.05 * jax.random.normal(jax.random.fold_in(_tk, 500 + 4), (1000, 16), jnp.float32)
        tbl_5 = 0.05 * jax.random.normal(jax.random.fold_in(_tk, 500 + 5), (1000, 16), jnp.float32)
        tbl_6 = 0.05 * jax.random.normal(jax.random.fold_in(_tk, 500 + 6), (125000, 16), jnp.float32)
        tbl_7 = 0.05 * jax.random.normal(jax.random.fold_in(_tk, 500 + 7), (1000, 16), jnp.float32)
        tbl_8 = 0.05 * jax.random.normal(jax.random.fold_in(_tk, 500 + 8), (125000, 16), jnp.float32)
        tbl_9 = 0.05 * jax.random.normal(jax.random.fold_in(_tk, 500 + 9), (1250, 16), jnp.float32)
        tbl_10 = 0.05 * jax.random.normal(jax.random.fold_in(_tk, 500 + 10), (12500, 16), jnp.float32)
        tbl_11 = 0.05 * jax.random.normal(jax.random.fold_in(_tk, 500 + 11), (1000, 16), jnp.float32)
        tbl_12 = 0.05 * jax.random.normal(jax.random.fold_in(_tk, 500 + 12), (12500, 16), jnp.float32)
        tbl_13 = 0.05 * jax.random.normal(jax.random.fold_in(_tk, 500 + 13), (125000, 16), jnp.float32)
        tbl_14 = 0.05 * jax.random.normal(jax.random.fold_in(_tk, 500 + 14), (125000, 16), jnp.float32)
        tbl_15 = 0.05 * jax.random.normal(jax.random.fold_in(_tk, 500 + 15), (1250, 16), jnp.float32)
        tbl_16 = 0.05 * jax.random.normal(jax.random.fold_in(_tk, 500 + 16), (1000, 16), jnp.float32)
        tbl_17 = 0.05 * jax.random.normal(jax.random.fold_in(_tk, 500 + 17), (12500, 16), jnp.float32)
        tbl_18 = 0.05 * jax.random.normal(jax.random.fold_in(_tk, 500 + 18), (1250, 16), jnp.float32)
        tbl_19 = 0.05 * jax.random.normal(jax.random.fold_in(_tk, 500 + 19), (12500, 16), jnp.float32)
        tbl_20 = 0.05 * jax.random.normal(jax.random.fold_in(_tk, 500 + 20), (12500, 16), jnp.float32)
        tbl_21 = 0.05 * jax.random.normal(jax.random.fold_in(_tk, 500 + 21), (1000, 16), jnp.float32)
        tbl_22 = 0.05 * jax.random.normal(jax.random.fold_in(_tk, 500 + 22), (1000, 16), jnp.float32)
        tbl_23 = 0.05 * jax.random.normal(jax.random.fold_in(_tk, 500 + 23), (1250, 16), jnp.float32)
        tbl_24 = 0.05 * jax.random.normal(jax.random.fold_in(_tk, 500 + 24), (1000, 16), jnp.float32)
        tbl_25 = 0.05 * jax.random.normal(jax.random.fold_in(_tk, 500 + 25), (1000, 16), jnp.float32)
        tbl_26 = 0.05 * jax.random.normal(jax.random.fold_in(_tk, 500 + 26), (1000, 16), jnp.float32)
        tbl_27 = 0.05 * jax.random.normal(jax.random.fold_in(_tk, 500 + 27), (1000, 16), jnp.float32)
        tbl_28 = 0.05 * jax.random.normal(jax.random.fold_in(_tk, 500 + 28), (1000, 16), jnp.float32)
        tbl_29 = 0.05 * jax.random.normal(jax.random.fold_in(_tk, 500 + 29), (12500, 16), jnp.float32)
        tbl_30 = 0.05 * jax.random.normal(jax.random.fold_in(_tk, 500 + 30), (125000, 16), jnp.float32)
        tbl_31 = 0.05 * jax.random.normal(jax.random.fold_in(_tk, 500 + 31), (1000, 16), jnp.float32)
        tbl_32 = 0.05 * jax.random.normal(jax.random.fold_in(_tk, 500 + 32), (125000, 16), jnp.float32)
        tbl_33 = 0.05 * jax.random.normal(jax.random.fold_in(_tk, 500 + 33), (125000, 16), jnp.float32)
        tbl_34 = 0.05 * jax.random.normal(jax.random.fold_in(_tk, 500 + 34), (1000, 16), jnp.float32)
        tbl_35 = 0.05 * jax.random.normal(jax.random.fold_in(_tk, 500 + 35), (12500, 16), jnp.float32)
        tbl_36 = 0.05 * jax.random.normal(jax.random.fold_in(_tk, 500 + 36), (1250, 16), jnp.float32)
        tbl_37 = 0.05 * jax.random.normal(jax.random.fold_in(_tk, 500 + 37), (125000, 16), jnp.float32)
        tbl_38 = 0.05 * jax.random.normal(jax.random.fold_in(_tk, 500 + 38), (125000, 16), jnp.float32)
        _rk = jax.random.fold_in(_tk, 7)
        W_top1 = 0.0606339 * jax.random.normal(jax.random.fold_in(_tk, 801), (272, 512), jnp.float32)
        W_top2 = 0.0441942 * jax.random.normal(jax.random.fold_in(_tk, 802), (512, 256), jnp.float32)
        W_top3 = 0.0625 * jax.random.normal(jax.random.fold_in(_tk, 803), (256, 1), jnp.float32)
        b_top1 = jnp.zeros((512,), jnp.float32)
        b_top2 = jnp.zeros((256,), jnp.float32)
        return (dense_ctx, ids, tbl_0, tbl_1, tbl_2, tbl_3, tbl_4, tbl_5, tbl_6, tbl_7, tbl_8, tbl_9, tbl_10, tbl_11, tbl_12, tbl_13, tbl_14, tbl_15, tbl_16, tbl_17, tbl_18, tbl_19, tbl_20, tbl_21, tbl_22, tbl_23, tbl_24, tbl_25, tbl_26, tbl_27, tbl_28, tbl_29, tbl_30, tbl_31, tbl_32, tbl_33, tbl_34, tbl_35, tbl_36, tbl_37, tbl_38, W_top1, b_top1, W_top2, b_top2, W_top3)
    dense_ctx, ids, tbl_0, tbl_1, tbl_2, tbl_3, tbl_4, tbl_5, tbl_6, tbl_7, tbl_8, tbl_9, tbl_10, tbl_11, tbl_12, tbl_13, tbl_14, tbl_15, tbl_16, tbl_17, tbl_18, tbl_19, tbl_20, tbl_21, tbl_22, tbl_23, tbl_24, tbl_25, tbl_26, tbl_27, tbl_28, tbl_29, tbl_30, tbl_31, tbl_32, tbl_33, tbl_34, tbl_35, tbl_36, tbl_37, tbl_38, W_top1, b_top1, W_top2, b_top2, W_top3 = _rec_inputs()

    def _L0_rec_setup():
        import jax, jax.numpy as jnp
        import numpy as np
        B, F0, D = (256, 39, 16)
        LAYER_SIZES = [128, 128, 128]
        key = jax.random.key(seed)
        ks = jax.random.split(key, 1 + 2 * len(LAYER_SIZES))
        inputs = jax.random.normal(ks[0], (B, F0, D), dtype=jnp.float32)
        out = {'inputs': inputs}
        field_nums = [F0]
        for i, size in enumerate(LAYER_SIZES):
            fk = field_nums[-1]
            fan_in = F0 * fk
            scale = np.sqrt(2.0 / (fan_in + size)).astype(np.float32)
            out[f'w{i}'] = jax.random.normal(ks[1 + 2 * i], (F0, fk, size), dtype=jnp.float32) * scale
            out[f'b{i}'] = jnp.zeros((size,), dtype=jnp.float32)
            field_nums.append(size // 2)
        return out
    _L0_rec_all = _L0_rec_setup()
    _L0_rec_in = {k: v for k, v in _L0_rec_all.items() if k in ('w0', 'w1', 'w2', 'b0', 'b1', 'b2')}
    del _L0_rec_all
    return {'dense_ctx': dense_ctx, 'ids': ids, 'tbl_0': tbl_0, 'tbl_1': tbl_1, 'tbl_2': tbl_2, 'tbl_3': tbl_3, 'tbl_4': tbl_4, 'tbl_5': tbl_5, 'tbl_6': tbl_6, 'tbl_7': tbl_7, 'tbl_8': tbl_8, 'tbl_9': tbl_9, 'tbl_10': tbl_10, 'tbl_11': tbl_11, 'tbl_12': tbl_12, 'tbl_13': tbl_13, 'tbl_14': tbl_14, 'tbl_15': tbl_15, 'tbl_16': tbl_16, 'tbl_17': tbl_17, 'tbl_18': tbl_18, 'tbl_19': tbl_19, 'tbl_20': tbl_20, 'tbl_21': tbl_21, 'tbl_22': tbl_22, 'tbl_23': tbl_23, 'tbl_24': tbl_24, 'tbl_25': tbl_25, 'tbl_26': tbl_26, 'tbl_27': tbl_27, 'tbl_28': tbl_28, 'tbl_29': tbl_29, 'tbl_30': tbl_30, 'tbl_31': tbl_31, 'tbl_32': tbl_32, 'tbl_33': tbl_33, 'tbl_34': tbl_34, 'tbl_35': tbl_35, 'tbl_36': tbl_36, 'tbl_37': tbl_37, 'tbl_38': tbl_38, 'W_top1': W_top1, 'b_top1': b_top1, 'W_top2': W_top2, 'b_top2': b_top2, 'W_top3': W_top3, 'L0_rec_w0': _L0_rec_in['w0'], 'L0_rec_w1': _L0_rec_in['w1'], 'L0_rec_w2': _L0_rec_in['w2'], 'L0_rec_b0': _L0_rec_in['b0'], 'L0_rec_b1': _L0_rec_in['b1'], 'L0_rec_b2': _L0_rec_in['b2']}

def reference(dense_ctx, ids, tbl_0, tbl_1, tbl_2, tbl_3, tbl_4, tbl_5, tbl_6, tbl_7, tbl_8, tbl_9, tbl_10, tbl_11, tbl_12, tbl_13, tbl_14, tbl_15, tbl_16, tbl_17, tbl_18, tbl_19, tbl_20, tbl_21, tbl_22, tbl_23, tbl_24, tbl_25, tbl_26, tbl_27, tbl_28, tbl_29, tbl_30, tbl_31, tbl_32, tbl_33, tbl_34, tbl_35, tbl_36, tbl_37, tbl_38, W_top1, b_top1, W_top2, b_top2, W_top3, L0_rec_w0, L0_rec_w1, L0_rec_w2, L0_rec_b0, L0_rec_b1, L0_rec_b2):
    import jax
    import jax.numpy as jnp

    def _L0_rec_ref(inputs, w0, w1, w2, b0, b1, b2):
        import jax, jax.numpy as jnp
        import numpy as np
        B, F0, D = (256, 39, 16)
        LAYER_SIZES = [128, 128, 128]
        x0 = inputs
        xk = inputs
        params = [(w0, b0), (w1, b1), (w2, b2)]
        n_layers = len(params)
        direct = []
        for idx, (W, b) in enumerate(params):
            z = jnp.einsum('bhd,bkd,hks->bsd', x0, xk, W) + b[None, :, None]
            z = jax.nn.relu(z)
            if idx != n_layers - 1:
                half = z.shape[1] // 2
                xk = z[:, :half, :]
                direct.append(z[:, half:, :])
            else:
                direct.append(z)
        logit = jnp.sum(jnp.concatenate(direct, axis=1), axis=-1)
        return logit
    e = jnp.stack([tbl_0[ids[:, 0]], tbl_1[ids[:, 1]], tbl_2[ids[:, 2]], tbl_3[ids[:, 3]], tbl_4[ids[:, 4]], tbl_5[ids[:, 5]], tbl_6[ids[:, 6]], tbl_7[ids[:, 7]], tbl_8[ids[:, 8]], tbl_9[ids[:, 9]], tbl_10[ids[:, 10]], tbl_11[ids[:, 11]], tbl_12[ids[:, 12]], tbl_13[ids[:, 13]], tbl_14[ids[:, 14]], tbl_15[ids[:, 15]], tbl_16[ids[:, 16]], tbl_17[ids[:, 17]], tbl_18[ids[:, 18]], tbl_19[ids[:, 19]], tbl_20[ids[:, 20]], tbl_21[ids[:, 21]], tbl_22[ids[:, 22]], tbl_23[ids[:, 23]], tbl_24[ids[:, 24]], tbl_25[ids[:, 25]], tbl_26[ids[:, 26]], tbl_27[ids[:, 27]], tbl_28[ids[:, 28]], tbl_29[ids[:, 29]], tbl_30[ids[:, 30]], tbl_31[ids[:, 31]], tbl_32[ids[:, 32]], tbl_33[ids[:, 33]], tbl_34[ids[:, 34]], tbl_35[ids[:, 35]], tbl_36[ids[:, 36]], tbl_37[ids[:, 37]], tbl_38[ids[:, 38]]], axis=1)
    z = _L0_rec_ref(e, L0_rec_w0, L0_rec_w1, L0_rec_w2, L0_rec_b0, L0_rec_b1, L0_rec_b2)
    z = z.reshape(z.shape[0], -1)
    h = jnp.concatenate([z, dense_ctx], axis=1)
    h = jnp.maximum(h @ W_top1 + b_top1, 0.0)
    h = jnp.maximum(h @ W_top2 + b_top2, 0.0)
    y = h @ W_top3
    return y

_drawn_inputs = setup_inputs


def setup_inputs(seed=0):
    import zlib

    import numpy as np

    out = dict(_drawn_inputs(seed))
    spreads = {'b_top1': (0.0, 2.0),
     'b_top2': (0.0, 2.0),
     'L0_rec_b0': (0.0, 0.339),
     'L0_rec_b1': (0.0, 0.537),
     'L0_rec_b2': (0.0, 0.8)}
    factors = {'tbl_0': 8.0,
     'tbl_1': 8.0,
     'tbl_2': 8.0,
     'tbl_3': 8.0,
     'tbl_4': 8.0,
     'tbl_5': 8.0,
     'tbl_6': 8.0,
     'tbl_7': 8.0,
     'tbl_8': 8.0,
     'tbl_9': 8.0,
     'tbl_10': 8.0,
     'tbl_11': 8.0,
     'tbl_12': 8.0,
     'tbl_13': 8.0,
     'tbl_14': 8.0,
     'tbl_15': 8.0,
     'tbl_16': 8.0,
     'tbl_17': 8.0,
     'tbl_18': 8.0,
     'tbl_19': 8.0,
     'tbl_20': 8.0,
     'tbl_21': 8.0,
     'tbl_22': 8.0,
     'tbl_23': 8.0,
     'tbl_24': 8.0,
     'tbl_25': 8.0,
     'tbl_26': 8.0,
     'tbl_27': 8.0,
     'tbl_28': 8.0,
     'tbl_29': 8.0,
     'tbl_30': 8.0,
     'tbl_31': 8.0,
     'tbl_32': 8.0,
     'tbl_33': 8.0,
     'tbl_34': 8.0,
     'tbl_35': 8.0,
     'tbl_36': 8.0,
     'tbl_37': 8.0,
     'tbl_38': 8.0,
     'L0_rec_w0': 8.0,
     'L0_rec_w1': 6.255,
     'L0_rec_w2': 4.996,
     'dense_ctx': 8.0}
    for name, (base, spread) in spreads.items():
        noise = np.random.default_rng([zlib.crc32(name.encode()), seed]).standard_normal(out[name].shape)
        drawn = base * np.exp(spread * noise) if base else spread * noise
        out[name] = jnp.asarray(drawn.astype(out[name].dtype))
    for name, factor in factors.items():
        out[name] = (out[name] * factor).astype(out[name].dtype)
    return out
```

```python
from contextlib import ExitStack

import concourse.bass as bass
from concourse import mybir

P = 128
F32 = mybir.dt.float32
I32 = mybir.dt.int32
ALU = mybir.AluOpType
ACT = mybir.ActivationFunctionType
AX = mybir.AxisListType

BATCH, FIELDS, DIM = 1024, 39, 16
SIZE = 128
HALF = SIZE // 2
DENSE, TOP1, TOP2 = 16, 512, 256

BT = P
NBT = BATCH // BT
DT = 4
COLS = DT * BT
TPB = DIM // DT
TILES = NBT * TPB

DELTAS = FIELDS // 2 + 1
REP0 = 3
ROWS0 = REP0 * FIELDS
CH0 = -(-DELTAS // REP0)
LAST0 = (DELTAS - REP0 * (CH0 - 1)) * FIELDS
R, C = 8, 16
NI = -(-FIELDS // R)
NJ = HALF // C
CHK = NI * NJ
PER_STEP = CH0 + 2 * CHK

RING = 6
T_SLOTS = 4
A_SLOTS = 4


def layers_of(step):
    return [(layer, step - layer) for layer in range(3) if 0 <= step - layer < TILES]


def count_of(layer):
    return CH0 if layer == 0 else CHK


def slot_of(layer, c):
    return (c + (0, CH0, CH0 + CHK)[layer]) % RING


def number_products():
    first, back, last, n = {}, {}, {}, 0
    for step in range(TILES + 2):
        for layer, _ in layers_of(step):
            first[step, layer] = n
            for c in range(count_of(layer)):
                s = slot_of(layer, c)
                back[step, layer, c] = n - last[s] if s in last else None
                last[s] = n
                n += 1
    return first, back


FIRST, BACK = number_products()


def known(i):
    return type(i) is int


def tile_exists(i, j, lag):
    return not known(i) or 0 <= TPB * i + j - lag < TILES


def product_number(i, j, layer, c=0):
    if known(i):
        return FIRST[TPB * i + j, layer] + c
    return (i - 1) * (TPB * PER_STEP) + (FIRST[TPB + j, layer] + c)


def product_back(i, j, layer, c):
    return BACK[(TPB * i + j if known(i) else TPB + j), layer, c]


for _s in range(TPB, TPB * (NBT - 1)):
    for _l in range(3):
        assert FIRST[_s, _l] == FIRST[TPB + _s % TPB, _l] + (_s // TPB - 1) * TPB * PER_STEP
        for _c in range(count_of(_l)):
            assert BACK[_s, _l, _c] == BACK[TPB + _s % TPB, _l, _c]


def turn(i, j, lag, slots):
    return i * (TPB // slots) + (j - lag) // slots


def build(nc, tables, ids, ident, w0a, w0b, w1, w2, biases, dense_t, wt1, wt1d, wt2, wt3, out):
    ctx = ExitStack()
    with ctx:
        def sb(name, shape, dt=F32):
            return ctx.enter_context(nc.sbuf_tensor(name, shape, dt))

        def pb(name, shape):
            return ctx.enter_context(nc.psum_tensor(name, shape, F32))

        def sem(name):
            return ctx.enter_context(nc.semaphore(name))

        id_sb = sb("id_sb", [P, P])
        w0_sb = sb("w0_sb", [ROWS0, CH0, SIZE])
        w0b_sb = sb("w0b_sb", [ROWS0, CH0, SIZE])
        w1_sb = sb("w1_sb", [P, CHK, SIZE])
        w2_sb = sb("w2_sb", [P, CHK, SIZE])
        bias_sb = sb("bias_sb", [P, 9])
        dense_sb = sb("dense_sb", [DENSE, BATCH])
        wt1_sb = sb("wt1_sb", [P, 2, TOP1])
        wt1d_sb = sb("wt1d_sb", [DENSE, TOP1])
        wt2_sb = sb("wt2_sb", [P, TOP1 // P, TOP2])
        wt3_sb = sb("wt3_sb", [P, TOP2 // P])
        idx = sb("idx", [P, FIELDS], I32)
        gathered = sb("gathered", [P, FIELDS, DIM])
        emb = sb("emb", [P, DIM, ROWS0])
        x0 = sb("x0", [ROWS0, T_SLOTS, COLS])
        x0_rot = sb("x0_rot", [ROWS0, 2, CH0, COLS])
        x0_spread = sb("x0_spread", [P, A_SLOTS, NI, COLS])
        x1 = sb("x1", [HALF, 2, COLS])
        x2 = sb("x2", [P, 2, COLS])
        x1_spread = sb("x1_spread", [P, 2, NJ, COLS])
        x2_spread = sb("x2_spread", [P, 2, NJ, COLS])
        prod = sb("prod", [P, RING, COLS])
        direct = sb("direct", [P, 4, COLS])
        direct2 = sb("direct2", [P, 2, COLS])
        part = sb("part", [P, 2, BT, TPB])
        pooled = sb("pooled", [P, 2, BT])
        h1 = sb("h1", [P, TOP1 // P, BT])
        h2 = sb("h2", [P, TOP2 // P, BT])
        y = sb("y", [1, BATCH])

        z = [pb(f"z{layer}", [SIZE, COLS]) for layer in range(3)]
        turned = pb("turned", [P, 2, COLS])
        h1_ps = pb("h1_ps", [P, TOP1 // P, BT])
        h2_ps = pb("h2_ps", [P, TOP2 // P, BT])
        y_ps = pb("y_ps", [1, COLS])

        w0_landed = sem("w0_landed")
        w_landed = sem("w_landed")
        bias_landed = sem("bias_landed")
        id_landed = sem("id_landed")
        top_landed = sem("top_landed")
        w0_summed = sem("w0_summed")
        idx_landed = sem("idx_landed")
        rows_free = sem("rows_free")
        ids_there = sem("ids_there")
        rows_gathered = sem("rows_gathered")
        emb_ready = sem("emb_ready")
        tile_turned = sem("tile_turned")
        x0_ready = sem("x0_ready")
        rot_landed = [sem(f"rot_landed{s}") for s in range(2)]
        spread_landed = [sem(f"spread_landed{s}") for s in range(A_SLOTS)]
        x1_spread_landed = [sem(f"x1_spread_landed{s}") for s in range(2)]
        x2_spread_landed = [sem(f"x2_spread_landed{s}") for s in range(2)]
        x0_saved = sem("x0_saved")
        x1_saved = sem("x1_saved")
        x2_saved = sem("x2_saved")
        product_made = sem("product_made")
        product_used = sem("product_used")
        z_done = [sem(f"z{layer}_done") for layer in range(3)]
        x1_ready = sem("x1_ready")
        x2_ready = sem("x2_ready")
        direct_ready = [sem(f"direct{layer}_ready") for layer in range(3)]
        direct_summed = sem("direct_summed")
        direct2_summed = sem("direct2_summed")
        pooled_ready = sem("pooled_ready")
        h1_done = sem("h1_done")
        h1_ready = sem("h1_ready")
        h2_done = sem("h2_done")
        h2_ready = sem("h2_ready")
        y_done = sem("y_done")
        y_ready = sem("y_ready")
        out_written = sem("out_written")

        x0_dram = nc.dram_tensor("x0_dram", (T_SLOTS, 2 * FIELDS, COLS), F32, kind="Internal")
        x1_dram = nc.dram_tensor("x1_dram", (2, HALF, COLS), F32, kind="Internal")
        x2_dram = nc.dram_tensor("x2_dram", (2, HALF, COLS), F32, kind="Internal")

        block = ctx.enter_context(nc.Block())

        @block.sync
        def _(sp):
            sp.dma_start(id_sb[:], ident).then_inc(id_landed, 16)
            sp.dma_start(bias_sb[:], biases).then_inc(bias_landed, 16)
            sp.dma_start(w0_sb[:], w0a).then_inc(w0_landed, 16)
            sp.dma_start(w0b_sb[:], w0b).then_inc(w0_landed, 16)
            sp.dma_start(w1_sb[:], w1).then_inc(w_landed, 16)
            sp.dma_start(w2_sb[:], w2).then_inc(w_landed, 16)
            for dst, src in ((dense_sb, dense_t), (wt1_sb, wt1), (wt1d_sb, wt1d), (wt2_sb, wt2), (wt3_sb, wt3)):
                sp.dma_start(dst[:], src).then_inc(top_landed, 16)

            def save_x0(i, j, lag):
                slot = (j - lag) % T_SLOTS
                sp.wait_ge(x0_ready, TPB * i + j - lag + 1)
                sp.dma_start(x0_dram[slot], x0[0:2 * FIELDS, slot, :]).then_inc(x0_saved, 16)

            def rotate_x0(i, j, lag):
                slot, r_slot = (j - lag) % T_SLOTS, (j - lag) % 2
                sp.wait_ge(x0_saved, 16 * (TPB * i + j - lag + 1))
                for r in range(REP0):
                    chunks = CH0 if r < LAST0 // FIELDS else CH0 - 1
                    src = bass.AP(x0_dram, (slot * 2 * FIELDS + r) * COLS,
                                  [[COLS, FIELDS], [REP0 * COLS, chunks], [1, COLS]])
                    sp.dma_start(x0_rot[r * FIELDS:(r + 1) * FIELDS, r_slot, 0:chunks, :],
                                 src).then_inc(rot_landed[r_slot], 16)

            def spread_x0(i, j, lag):
                slot = (j - lag) % T_SLOTS
                src = bass.AP(x0_dram, slot * 2 * FIELDS * COLS, [[0, C], [NI * COLS, R], [1, NI * COLS]])
                sp.dma_start(x0_spread[:, slot, :, :].rearrange("p i n -> p (i n)"),
                             src).then_inc(spread_landed[slot], 16)

            def save_half(i, j, lag, x, ready, dram, saved):
                slot = (j - lag) % 2
                sp.wait_ge(ready, TPB * i + j - lag + 1)
                sp.dma_start(dram[slot], x[:, slot, :]).then_inc(saved, 16)

            def spread_half(i, j, lag, dram, saved, spread, landed):
                slot = (j - lag) % 2
                sp.wait_ge(saved, 16 * (TPB * i + j - lag + 1))
                src = bass.AP(dram, slot * HALF * COLS, [[NJ * COLS, C], [0, R], [1, NJ * COLS]])
                sp.dma_start(spread[:, slot, :, :].rearrange("p j n -> p (j n)"),
                             src).then_inc(landed[slot], 16)

            def step(i, j):
                if tile_exists(i, j, -1):
                    save_x0(i, j, -1)
                if tile_exists(i, j, 0):
                    save_half(i, j, 0, x1, x1_ready, x1_dram, x1_saved)
                if tile_exists(i, j, -1):
                    rotate_x0(i, j, -1)
                if tile_exists(i, j, 0):
                    spread_half(i, j, 0, x1_dram, x1_saved, x1_spread, x1_spread_landed)
                if tile_exists(i, j, -1):
                    spread_x0(i, j, -1)
                if tile_exists(i, j, 1):
                    save_half(i, j, 1, x2[HALF:P], x2_ready, x2_dram, x2_saved)
                    spread_half(i, j, 1, x2_dram, x2_saved, x2_spread, x2_spread_landed)

            save_x0(0, 0, 0)
            rotate_x0(0, 0, 0)
            spread_x0(0, 0, 0)
            for j in range(TPB):
                step(0, j)
            with sp.Fori(1, NBT - 1) as i:
                for j in range(TPB):
                    step(i, j)
            for j in range(TPB + 1):
                step(NBT - 1, j)
            sp.wait_ge(y_ready, NBT)
            sp.dma_start(out.rearrange("b o -> o b"), y[:]).then_inc(out_written, 16)
            sp.wait_ge(out_written, 16)

        @block.gpsimd
        def _(pool):
            def gather(b):
                if not known(b) or b > 0:
                    pool.wait_ge(emb_ready, REP0 * b)
                    pool.sem_inc(rows_free, 1)
                pool.dma_start(idx[:], ids[b]).then_inc(idx_landed, 16)
                pool.wait_ge(idx_landed, 16 * (b + 1))
                pool.sem_inc(ids_there, 1)
                for f in range(FIELDS):
                    pool.indirect_dma_start(gathered[:, f, :], None, tables[f],
                                            bass.IndirectOffsetOnAxis(idx[:, f:f + 1], 0)
                                            ).then_inc(rows_gathered, 16)

            gather(0)
            with pool.Fori(1, NBT) as b:
                gather(b)

        @block.tensor
        def _(pe):
            def turn_tile(i, j, lag):
                q, bank = (j - lag) % TPB, (j - lag) % 2
                pe.wait_ge(emb_ready, REP0 * (turn(i, j, lag, TPB) + 1))
                if tile_exists(i, j, lag + 2):
                    pe.wait_ge(x0_ready, TPB * i + j - lag - 1)
                for d in range(DT):
                    mm = nc.tensor.transpose(turned[0:ROWS0, bank, d * BT:(d + 1) * BT],
                                             emb[:, q * DT + d, :], id_sb[:])
                mm.then_inc(tile_turned, 1)

            def interact(i, j, layer):
                t = TPB * i + j - layer
                if tile_exists(i, j, layer + 1):
                    pe.wait_ge(direct_ready[layer], t)
                    if layer < 2:
                        pe.wait_ge((x1_ready, x2_ready)[layer], t)
                for c in range(count_of(layer)):
                    rows, w = P, (w0_sb, w1_sb, w2_sb)[layer]
                    if layer == 0:
                        rows = ROWS0 if c < CH0 - 1 else LAST0
                    pe.wait_ge(product_made, product_number(i, j, layer, c) + 1)
                    mm = nc.tensor.matmul(z[layer][:], w[0:rows, c, :], prod[0:rows, slot_of(layer, c), :],
                                          start=(c == 0), stop=(c == count_of(layer) - 1))
                    mm.then_inc(product_used, 1)
                pe.wait_ge(product_used, product_number(i, j, layer, count_of(layer)))
                pe.sem_inc(z_done[layer], 1)

            def top1(b):
                pe.wait_ge(pooled_ready, 2 * (b + 1))
                if not known(b) or b > 0:
                    pe.wait_ge(h1_ready, 4 * b)
                for m in range(TOP1 // P):
                    for k in range(2):
                        nc.tensor.matmul(h1_ps[:, m, :], wt1_sb[:, k, m * P:(m + 1) * P], pooled[:, k, :],
                                         start=(k == 0), stop=False)
                    mm = nc.tensor.matmul(h1_ps[:, m, :], wt1d_sb[:, m * P:(m + 1) * P],
                                          dense_sb[:, bass.ds(b * BT, BT)], start=False, stop=True)
                mm.then_inc(h1_done, 1)

            def top2(b):
                pe.wait_ge(h1_ready, 4 * (b + 1))
                if not known(b) or b > 0:
                    pe.wait_ge(h2_ready, 2 * b)
                for m in range(TOP2 // P):
                    for k in range(TOP1 // P):
                        mm = nc.tensor.matmul(h2_ps[:, m, :], wt2_sb[:, k, m * P:(m + 1) * P], h1[:, k, :],
                                              start=(k == 0), stop=(k == TOP1 // P - 1))
                mm.then_inc(h2_done, 1)

            def top3(b):
                pe.wait_ge(h2_ready, 2 * (b + 1))
                if not known(b) or b > 0:
                    pe.wait_ge(y_ready, b)
                for k in range(TOP2 // P):
                    mm = nc.tensor.matmul(y_ps[:, 0:BT], wt3_sb[:, k:k + 1], h2[:, k, :],
                                          start=(k == 0), stop=(k == TOP2 // P - 1))
                mm.then_inc(y_done, 1)

            def step(i, j):
                top = (not known(i) or i > 0)
                if tile_exists(i, j, 0):
                    interact(i, j, 0)
                if tile_exists(i, j, -2):
                    turn_tile(i, j, -2)
                if top and j == 3:
                    top3(i - 1)
                if tile_exists(i, j, 1):
                    interact(i, j, 1)
                if top and j == 2:
                    top1(i - 1)
                if tile_exists(i, j, 2):
                    interact(i, j, 2)
                if top and j == 2:
                    top2(i - 1)

            pe.wait_ge(id_landed, 16)
            turn_tile(0, 0, 0)
            turn_tile(0, 1, 0)
            pe.wait_ge(w0_summed, 1)
            pe.wait_ge(w_landed, 32)
            pe.wait_ge(top_landed, 80)
            for j in range(TPB):
                step(0, j)
            with pe.Fori(1, NBT - 1) as i:
                for j in range(TPB):
                    step(i, j)
            for j in range(TPB + 2):
                if j < TPB:
                    step(NBT - 1, j)
                elif j == TPB:
                    interact(NBT - 1, j, 1)
                    interact(NBT - 1, j, 2)
                else:
                    interact(NBT - 1, j, 2)
            top1(NBT - 1)
            top2(NBT - 1)
            top3(NBT - 1)

        @block.vector
        def _(dve):
            def products(i, j, layer):
                lag = layer
                if layer == 0:
                    dve.wait_ge(rot_landed[j % 2], 16 * REP0 * (turn(i, j, 0, 2) + 1))
                else:
                    a = (j - lag) % A_SLOTS
                    dve.wait_ge(spread_landed[a], 16 * (turn(i, j, lag, A_SLOTS) + 1))
                    b = (j - lag) % 2
                    landed = (x1_spread_landed, x2_spread_landed)[layer - 1][b]
                    dve.wait_ge(landed, 16 * (turn(i, j, lag, 2) + 1))
                for c in range(count_of(layer)):
                    back = product_back(i, j, layer, c)
                    if back is not None:
                        dve.wait_ge(product_used, product_number(i, j, layer, c) - back + 1)
                    if layer == 0:
                        rows = ROWS0 if c < CH0 - 1 else LAST0
                        left, right = x0[0:rows, j % T_SLOTS, :], x0_rot[0:rows, j % 2, c, :]
                    else:
                        rows = P
                        spread = (x1_spread, x2_spread)[layer - 1]
                        left, right = x0_spread[:, a, c // NJ, :], spread[:, b, c % NJ, :]
                    nc.vector.tensor_tensor(prod[0:rows, slot_of(layer, c), :], left, right,
                                            ALU.mult).then_inc(product_made, 1)

            def sum_direct(i, j):
                t = TPB * i + j - 2
                dve.wait_ge(direct_ready[0], t + 1)
                dve.wait_ge(direct_ready[1], t + 1)
                nc.vector.tensor_reduce(part[:, 0, :, (j - 2) % TPB],
                                        direct[:, (j - 2) % 4, :].rearrange("p (d b) -> p b d", d=DT),
                                        AX.X, ALU.add).then_inc(direct_summed, 1)

            def sum_direct2(i, j):
                t = TPB * i + j - 3
                dve.wait_ge(direct_ready[2], t + 1)
                nc.vector.tensor_reduce(part[:, 1, :, (j - 3) % TPB],
                                        direct2[:, (j - 3) % 2, :].rearrange("p (d b) -> p b d", d=DT),
                                        AX.X, ALU.add).then_inc(direct2_summed, 1)

            def pool_batch_tile(b, layer01):
                if layer01:
                    dve.wait_ge(direct_summed, TPB * (b + 1))
                else:
                    dve.wait_ge(direct2_summed, TPB * (b + 1))
                if not known(b) or b > 0:
                    dve.wait_ge(h1_done, b)
                k = 0 if layer01 else 1
                nc.vector.tensor_reduce(pooled[:, k, :], part[:, k, :, :],
                                        AX.X, ALU.add).then_inc(pooled_ready, 1)

            def step(i, j):
                top = (not known(i) or i > 0)
                if tile_exists(i, j, 0):
                    products(i, j, 0)
                if tile_exists(i, j, 2):
                    sum_direct(i, j)
                    if j == 1 and top:
                        pool_batch_tile(i - 1, True)
                if tile_exists(i, j, 3):
                    sum_direct2(i, j)
                    if j == 2 and top:
                        pool_batch_tile(i - 1, False)
                if tile_exists(i, j, 1):
                    products(i, j, 1)
                if tile_exists(i, j, 2):
                    products(i, j, 2)

            dve.wait_ge(w0_landed, 32)
            nc.vector.tensor_tensor(w0_sb[:], w0_sb[:], w0b_sb[:], ALU.add).then_inc(w0_summed, 1)
            for j in range(TPB):
                step(0, j)
            with dve.Fori(1, NBT - 1) as i:
                for j in range(TPB):
                    step(i, j)
            for j in range(TPB):
                step(NBT - 1, j)
            last = NBT - 1
            sum_direct(last, 4)
            sum_direct2(last, 4)
            products(last, 4, 1)
            products(last, 4, 2)
            sum_direct(last, 5)
            pool_batch_tile(last, True)
            sum_direct2(last, 5)
            products(last, 5, 2)
            sum_direct2(last, 6)
            pool_batch_tile(last, False)

        @block.scalar
        def _(act):
            def leave(i, j, layer):
                t, jt = TPB * i + j - layer, j - layer
                act.wait_ge(z_done[layer], t + 1)
                zl, b = z[layer], bias_sb[:, layer:layer + 1]
                if layer == 2:
                    nc.scalar.activation(direct2[:, jt % 2, :], zl[:], ACT.Relu,
                                         bias=b).then_inc(direct_ready[2], 1)
                    return
                on = slice(0, HALF) if layer == 0 else slice(HALF, P)
                stay = slice(HALF, P) if layer == 0 else slice(0, HALF)
                x, ready = ((x1, x1_ready), (x2, x2_ready))[layer]
                nc.scalar.activation(x[on, jt % 2, :], zl[on, :], ACT.Relu,
                                     bias=b[on, :]).then_inc(ready, 1)
                nc.scalar.activation(direct[stay, jt % 4, :], zl[stay, :], ACT.Relu,
                                     bias=b[stay, :]).then_inc(direct_ready[layer], 1)

            def order_rows(b):
                act.wait_ge(rows_gathered, 16 * FIELDS * (b + 1))
                if not known(b) or b > 0:
                    act.wait_ge(tile_turned, TPB * b)
                for r in range(REP0):
                    nc.scalar.copy(emb[:, :, r * FIELDS:(r + 1) * FIELDS],
                                   gathered[:].rearrange("p f d -> p d f")).then_inc(emb_ready, 1)

            def take_x0(i, j, lag):
                t = TPB * i + j - lag
                act.wait_ge(tile_turned, t + 1)
                nc.scalar.copy(x0[:, (j - lag) % T_SLOTS, :],
                               turned[0:ROWS0, (j - lag) % 2, :]).then_inc(x0_ready, 1)

            def relu_top(b, src, dst, chunks, done, ready, col, read, reads):
                act.wait_ge(done, b + 1)
                if not known(b) or b > 0:
                    act.wait_ge(read, reads * b)
                for m in range(chunks):
                    nc.scalar.activation(dst[:, m, :], src[:, m, :], ACT.Relu,
                                         bias=bias_sb[:, col + m:col + m + 1]).then_inc(ready, 1)

            def relu_top1(b):
                relu_top(b, h1_ps, h1, TOP1 // P, h1_done, h1_ready, 3, h2_done, 1)

            def relu_top2(b):
                relu_top(b, h2_ps, h2, TOP2 // P, h2_done, h2_ready, 3 + TOP1 // P, y_done, 1)

            def take_y(b):
                act.wait_ge(y_done, b + 1)
                nc.scalar.copy(y[:, bass.ds(b * BT, BT)], y_ps[:, 0:BT]).then_inc(y_ready, 1)

            def step(i, j):
                top = (not known(i) or i > 0)
                if tile_exists(i, j, 0):
                    leave(i, j, 0)
                if tile_exists(i, j, -2):
                    take_x0(i, j, -2)
                if j == 1 and (not known(i) or i < NBT - 1):
                    order_rows(i + 1)
                if top and j == 3:
                    take_y(i - 1)
                if tile_exists(i, j, 1):
                    leave(i, j, 1)
                if top and j == 2:
                    relu_top1(i - 1)
                if tile_exists(i, j, 2):
                    leave(i, j, 2)
                if top and j == 2:
                    relu_top2(i - 1)

            act.wait_ge(bias_landed, 16)
            order_rows(0)
            take_x0(0, 0, 0)
            take_x0(0, 1, 0)
            for j in range(TPB):
                step(0, j)
            with act.Fori(1, NBT - 1) as i:
                for j in range(TPB):
                    step(i, j)
            last = NBT - 1
            for j in range(TPB):
                step(last, j)
            leave(last, 4, 1)
            leave(last, 4, 2)
            leave(last, 5, 2)
            relu_top1(last)
            relu_top2(last)
            take_y(last)


def kernel(**inputs):
    import numpy as np
    import concourse.bacc as bacc
    from concourse.bass_utils import run_bass_kernel_spmd

    given = {k: np.asarray(v) for k, v in inputs.items()}

    w0 = given["L0_rec_w0"]
    w0a = np.zeros((ROWS0, CH0, SIZE), w0.dtype)
    w0b = np.zeros((ROWS0, CH0, SIZE), w0.dtype)
    h = np.arange(FIELDS)
    for delta in range(DELTAS):
        rows, c = slice(delta % REP0 * FIELDS, (delta % REP0 + 1) * FIELDS), delta // REP0
        w0a[rows, c] = w0[h, (h + delta) % FIELDS]
        if delta:
            w0b[rows, c] = w0[(h + delta) % FIELDS, h]

    def spread_weights(w):
        padded = np.zeros((R * NI, HALF, SIZE), w.dtype)
        padded[:FIELDS] = w
        return padded.reshape(R, NI, C, NJ, SIZE).transpose(2, 0, 1, 3, 4).reshape(P, CHK, SIZE)

    def swap(w, axis):
        return np.concatenate([w.take(range(HALF, SIZE), axis), w.take(range(HALF), axis)], axis)

    def columns(v):
        return v.reshape(-1, P).T

    t1 = given["W_top1"]
    arrays = {
        "ids": given["ids"].reshape(NBT, BT, FIELDS),
        "ident": np.eye(P, dtype=np.float32),
        "w0a": w0a,
        "w0b": w0b,
        "w1": spread_weights(swap(given["L0_rec_w1"], 2)),
        "w2": spread_weights(given["L0_rec_w2"]),
        "biases": np.concatenate([columns(v) for v in (given["L0_rec_b0"], swap(given["L0_rec_b1"], 0),
                                                       given["L0_rec_b2"], given["b_top1"], given["b_top2"])], 1),
        "dense_t": given["dense_ctx"].T,
        "wt1": np.stack([np.concatenate([t1[HALF:2 * HALF], t1[:HALF]]), t1[P:2 * P]], 1),
        "wt1d": t1[2 * P:],
        "wt2": given["W_top2"].reshape(TOP1 // P, P, TOP2).transpose(1, 0, 2),
        "wt3": given["W_top3"].reshape(TOP2 // P, P).T,
    }
    for f in range(FIELDS):
        arrays[f"tbl_{f}"] = given[f"tbl_{f}"]
    arrays = {k: np.ascontiguousarray(v) for k, v in arrays.items()}

    nc = bacc.Bacc("TRN2", target_bir_lowering=False, num_devices=1)
    aps = {k: nc.dram_tensor(k, v.shape, mybir.dt.from_np(v.dtype), kind="ExternalInput").ap()
           for k, v in arrays.items()}
    out = nc.dram_tensor("out", (BATCH, 1), F32, kind="ExternalOutput").ap()
    tables = [aps.pop(f"tbl_{f}") for f in range(FIELDS)]
    build(nc, tables, out=out, **aps)
    r = run_bass_kernel_spmd(nc, [arrays], core_ids=[0])
    return r.results[0]["out"]
```

```python
from contextlib import ExitStack

import concourse.bass as bass
from concourse import mybir

P = 128
F32 = mybir.dt.float32
F32R = mybir.dt.float32r
I32 = mybir.dt.int32
ALU = mybir.AluOpType
ACT = mybir.ActivationFunctionType
AX = mybir.AxisListType

BATCH, FIELDS, DIM = 1024, 39, 16
SIZE = 128
HALF = SIZE // 2
DENSE, TOP1, TOP2 = 16, 512, 256

BT = P
NBT = BATCH // BT
DT = 4
COLS = DT * BT
TPB = DIM // DT
TILES = NBT * TPB

DELTAS = FIELDS // 2 + 1
REP0 = 3
ROWS0 = REP0 * FIELDS
CH0 = -(-DELTAS // REP0)
R, C = 8, 16
NI = -(-FIELDS // R)
NJ = HALF // C
CHK = NI * NJ

WIDTH = 4
GROUPS = (-(-CH0 // WIDTH), CHK // WIDTH, CHK // WIDTH)
PLACE0 = (0, GROUPS[0], GROUPS[0] + GROUPS[1])
PER_STEP = sum(GROUPS)
SPLIT = (1, 3)
NSPLIT = len(SPLIT)
LO_LAG = 1
RING = 4
PARTS = 2
LEAVE = 2
X0_SLOTS = 2
X0_SAVED = 4
assert PER_STEP % RING == 0 and NSPLIT % PARTS == 0 and CHK % WIDTH == 0 and NJ % WIDTH == 0

WHOLE_CHUNKS = [c for c in range(CHK) if c // WIDTH not in SPLIT]
SPLIT_CHUNKS = [c for c in range(CHK) if c // WIDTH in SPLIT]


def chunks_of(layer, g):
    return range(WIDTH * g, min(WIDTH * g + WIDTH, CH0 if layer == 0 else CHK))


def is_split(layer, g):
    return layer > 0 and g in SPLIT


def slot_of(layer, g):
    return (PLACE0[layer] + g) % RING


def layers_of(step):
    return [(layer, step - layer) for layer in range(3) if 0 <= step - layer < TILES]


def number_groups():
    t = {k: {} for k in ("number", "split", "whole_held", "split_held", "part_held")}
    slots, parts, n = {}, [], 0
    for step in range(TILES + 2):
        for layer, _ in layers_of(step):
            for g in range(GROUPS[layer]):
                at, slot = (step, layer, g), slot_of(layer, g)
                t["number"][at], t["split"][at] = n, len(parts)
                if slot in slots:
                    kind, number = slots[slot]
                    t[kind][at] = number
                slots[slot] = ("whole_held", n)
                if is_split(layer, g):
                    if len(parts) >= PARTS:
                        t["part_held"][at] = parts[-PARTS]
                    slots[slot] = ("split_held", len(parts))
                    parts.append(n)
                n += 1
    return t


TABLE = number_groups()
GROWTH = {k: TPB * (2 * NSPLIT if k in ("split", "split_held") else PER_STEP) for k in TABLE}
for _k in TABLE:
    for _s, _l, _g in TABLE["number"]:
        if 2 * TPB <= _s < TPB * (NBT - 1):
            _now, _then = TABLE[_k].get((_s, _l, _g)), TABLE[_k].get((_s - TPB, _l, _g))
            assert _now == (None if _then is None else _then + GROWTH[_k])


def known(i):
    return type(i) is int


def tile_exists(i, j, lag):
    return not known(i) or 0 <= TPB * i + j - lag < TILES


def look_up(table, i, j, layer, g=0):
    if known(i):
        return TABLE[table].get((TPB * i + j, layer, g))
    first = TABLE[table].get((2 * TPB + j, layer, g))
    return None if first is None else (i - 2) * GROWTH[table] + first


def turn(i, j, lag, slots):
    return i * (TPB // slots) + (j - lag) // slots


def build(nc, tables, ids, ident, w0a, w0b, w1, w2, w1s, w2s, biases, dense_t, wt1, wt1d, wt2, wt3, out):
    ctx = ExitStack()
    with ctx:
        def sb(name, shape, dt=F32):
            return ctx.enter_context(nc.sbuf_tensor(name, shape, dt))

        def pb(name, shape):
            return ctx.enter_context(nc.psum_tensor(name, shape, F32))

        def sem(name):
            return ctx.enter_context(nc.semaphore(name))

        id_sb = sb("id_sb", [P, P])
        w0_sb = sb("w0_sb", [ROWS0, CH0, SIZE])
        w1_sb = sb("w1_sb", [P, len(WHOLE_CHUNKS), SIZE])
        w2_sb = sb("w2_sb", [P, len(WHOLE_CHUNKS), SIZE])
        w_hi = sb("w_hi", [P, 2, len(SPLIT_CHUNKS), SIZE], F32R)
        w_lo = sb("w_lo", [P, 2, len(SPLIT_CHUNKS), SIZE], F32R)
        bias_sb = sb("bias_sb", [P, 9])
        dense_sb = sb("dense_sb", [DENSE, BATCH])
        wt1_sb = sb("wt1_sb", [P, 2, TOP1])
        wt1d_sb = sb("wt1d_sb", [DENSE, TOP1])
        wt2_sb = sb("wt2_sb", [P, TOP1 // P, TOP2])
        wt3_sb = sb("wt3_sb", [P, TOP2 // P])
        idx = sb("idx", [P, FIELDS], I32)
        gathered = sb("gathered", [P, FIELDS, DIM])
        emb = sb("emb", [P, DIM, ROWS0])
        x0 = sb("x0", [ROWS0, X0_SLOTS, COLS])
        x0_rot = sb("x0_rot", [ROWS0, CH0, COLS])
        x0_spread = [sb(f"x0_spread{layer}", [P, NI, COLS]) for layer in (1, 2)]
        x1 = sb("x1", [HALF, COLS])
        x2 = sb("x2", [P, COLS])
        x_spread = [sb(f"x{layer}_spread", [P, NJ, COLS]) for layer in (1, 2)]
        prod = sb("prod", [P, RING, WIDTH, COLS])
        hi = sb("hi", [P, PARTS, WIDTH, COLS], F32R)
        lo = sb("lo", [P, PARTS, WIDTH, COLS], F32R)
        flat = prod[:].rearrange("p r c n -> p (r c n)")
        n_split = len(SPLIT_CHUNKS) * SIZE
        stage = flat[:, 0:2 * n_split].rearrange("p (l c n) -> p l c n", l=2, n=SIZE)
        w0b_sb = flat[0:ROWS0, 2 * n_split:2 * n_split + CH0 * SIZE].rearrange("p (c n) -> p c n", n=SIZE)
        direct = sb("direct", [P, 4, COLS])
        direct2 = sb("direct2", [P, 2, COLS])
        part = sb("part", [P, 2, BT, TPB])
        pooled = sb("pooled", [P, 2, BT])
        h1 = sb("h1", [P, TOP1 // P, BT])
        h2 = sb("h2", [P, TOP2 // P, BT])
        y = sb("y", [1, BATCH])

        z = [pb(f"z{layer}", [SIZE, COLS]) for layer in range(3)]
        turned = pb("turned", [P, 2, COLS])
        h1_ps = pb("h1_ps", [P, TOP1 // P, BT])
        h2_ps = pb("h2_ps", [P, TOP2 // P, BT])
        y_ps = pb("y_ps", [1, COLS])

        w0_landed = sem("w0_landed")
        w_landed = sem("w_landed")
        bias_landed = sem("bias_landed")
        id_landed = sem("id_landed")
        top_landed = sem("top_landed")
        stage_landed = sem("stage_landed")
        hi_weights = sem("hi_weights")
        w0_summed = sem("w0_summed")
        lo_weights = sem("lo_weights")
        idx_landed = sem("idx_landed")
        rot_free = sem("rot_free")
        spread_free = sem("spread_free")
        rows_free = sem("rows_free")
        ids_there = sem("ids_there")
        rows_gathered = sem("rows_gathered")
        emb_ready = sem("emb_ready")
        tile_turned = sem("tile_turned")
        x0_ready = sem("x0_ready")
        rot_landed = sem("rot_landed")
        spreads_landed = [sem(f"spreads{layer}_landed") for layer in (1, 2)]
        x0_saved = sem("x0_saved")
        x1_saved = sem("x1_saved")
        x2_saved = sem("x2_saved")
        group_made = sem("group_made")
        hi_made = sem("hi_made")
        lo_made = sem("lo_made")
        group_used = sem("group_used")
        x1_ready = sem("x1_ready")
        x2_ready = sem("x2_ready")
        direct_ready = [sem(f"direct{layer}_ready") for layer in range(3)]
        direct_summed = sem("direct_summed")
        direct2_summed = sem("direct2_summed")
        pooled_ready = sem("pooled_ready")
        h1_done = sem("h1_done")
        h1_ready = sem("h1_ready")
        h2_done = sem("h2_done")
        h2_ready = sem("h2_ready")
        y_done = sem("y_done")
        y_ready = sem("y_ready")
        out_written = sem("out_written")

        x0_dram = nc.dram_tensor("x0_dram", (X0_SAVED, 2 * FIELDS, COLS), F32, kind="Internal")
        x1_dram = nc.dram_tensor("x1_dram", (2, HALF, COLS), F32, kind="Internal")
        x2_dram = nc.dram_tensor("x2_dram", (2, HALF, COLS), F32, kind="Internal")

        block = ctx.enter_context(nc.Block())

        @block.sync
        def _(sp):
            sp.dma_start(id_sb[:], ident).then_inc(id_landed, 16)
            sp.dma_start(bias_sb[:], biases).then_inc(bias_landed, 16)
            sp.dma_start(w0_sb[:], w0a).then_inc(w0_landed, 16)
            sp.dma_start(w0b_sb, w0b).then_inc(w0_landed, 16)
            sp.dma_start(stage[:, 0], w1s).then_inc(stage_landed, 16)
            sp.dma_start(stage[:, 1], w2s).then_inc(stage_landed, 16)
            sp.dma_start(w1_sb[:], w1).then_inc(w_landed, 16)
            sp.dma_start(w2_sb[:], w2).then_inc(w_landed, 16)
            for dst, src in ((dense_sb, dense_t), (wt1_sb, wt1), (wt1d_sb, wt1d), (wt2_sb, wt2), (wt3_sb, wt3)):
                sp.dma_start(dst[:], src).then_inc(top_landed, 16)

            def save_x0(i, j, lag):
                sp.wait_ge(x0_ready, TPB * i + j - lag + 1)
                sp.dma_start(x0_dram[(j - lag) % X0_SAVED],
                             x0[0:2 * FIELDS, (j - lag) % X0_SLOTS, :]).then_inc(x0_saved, 16)

            def rotate_x0(i, j, lag):
                sp.wait_ge(x0_saved, 16 * (TPB * i + j - lag + 1))
                for r in range(REP0):
                    src = bass.AP(x0_dram, ((j - lag) % X0_SAVED * 2 * FIELDS + r) * COLS,
                                  [[COLS, FIELDS], [REP0 * COLS, CH0], [1, COLS]])
                    sp.dma_start(x0_rot[r * FIELDS:(r + 1) * FIELDS, :, :], src).then_inc(rot_landed, 16)

            def save_half(i, j, lag, x, ready, dram, saved):
                sp.wait_ge(ready, TPB * i + j - lag + 1)
                sp.dma_start(dram[(j - lag) % 2], x).then_inc(saved, 16)

            def spread(i, j, lag, layer):
                dram, saved = ((x1_dram, x1_saved), (x2_dram, x2_saved))[layer - 1]
                landed = spreads_landed[layer - 1]
                src = bass.AP(x0_dram, (j - lag) % X0_SAVED * 2 * FIELDS * COLS,
                              [[0, C], [NI * COLS, R], [1, NI * COLS]])
                sp.dma_start(x0_spread[layer - 1][:].rearrange("p i n -> p (i n)"), src).then_inc(landed, 16)
                sp.wait_ge(saved, 16 * (TPB * i + j - lag + 1))
                src = bass.AP(dram, (j - lag) % 2 * HALF * COLS, [[NJ * COLS, C], [0, R], [1, NJ * COLS]])
                sp.dma_start(x_spread[layer - 1][:].rearrange("p j n -> p (j n)"), src).then_inc(landed, 16)

            def step(i, j):
                if tile_exists(i, j, 2):
                    if tile_exists(i, j, 3):
                        sp.wait_ge(group_made, look_up("number", i, j, 0 if tile_exists(i, j, 0) else
                                                       1 if tile_exists(i, j, 1) else 2))
                    spread(i, j, 2, 2)
                if tile_exists(i, j, -1):
                    save_x0(i, j, -1)
                    sp.wait_ge(group_made, look_up("number", i, j, 0) + GROUPS[0])
                    sp.sem_inc(rot_free, 1)
                    rotate_x0(i, j, -1)
                if tile_exists(i, j, 0):
                    save_half(i, j, 0, x1[:], x1_ready, x1_dram, x1_saved)
                    if tile_exists(i, j, 1):
                        sp.wait_ge(group_made, look_up("number", i, j, 1) + GROUPS[1])
                        sp.sem_inc(spread_free, 1)
                    spread(i, j, 0, 1)
                if tile_exists(i, j, 1):
                    save_half(i, j, 1, x2[HALF:P], x2_ready, x2_dram, x2_saved)

            save_x0(0, 0, 0)
            rotate_x0(0, 0, 0)
            for j in range(TPB):
                step(0, j)
            with sp.Fori(1, NBT - 1) as i:
                for j in range(TPB):
                    step(i, j)
            for j in range(TPB + 2):
                step(NBT - 1, j)
            sp.wait_ge(y_ready, NBT)
            sp.dma_start(out.rearrange("b o -> o b"), y[:]).then_inc(out_written, 16)
            sp.wait_ge(out_written, 16)

        @block.gpsimd
        def _(pool):
            def gather(b):
                if not known(b) or b > 0:
                    pool.wait_ge(emb_ready, REP0 * b)
                    pool.sem_inc(rows_free, 1)
                pool.dma_start(idx[:], ids[b]).then_inc(idx_landed, 16)
                pool.wait_ge(idx_landed, 16 * (b + 1))
                pool.sem_inc(ids_there, 1)
                for f in range(FIELDS):
                    pool.indirect_dma_start(gathered[:, f, :], None, tables[f],
                                            bass.IndirectOffsetOnAxis(idx[:, f:f + 1], 0)
                                            ).then_inc(rows_gathered, 16)

            gather(0)
            with pool.Fori(1, NBT) as b:
                gather(b)

        @block.tensor
        def _(pe):
            def turn_tile(i, j, lag):
                q, bank = (j - lag) % TPB, (j - lag) % 2
                pe.wait_ge(emb_ready, REP0 * (turn(i, j, lag, TPB) + 1))
                if tile_exists(i, j, lag + 2):
                    pe.wait_ge(x0_ready, TPB * i + j - lag - 1)
                for d in range(DT):
                    mm = nc.tensor.transpose(turned[0:ROWS0, bank, d * BT:(d + 1) * BT],
                                             emb[:, q * DT + d, :], id_sb[:])
                mm.then_inc(tile_turned, 1)

            def interact(i, j, layer):
                t = TPB * i + j - layer
                if tile_exists(i, j, layer + 1):
                    pe.wait_ge(direct_ready[layer], t)
                    if layer < 2:
                        pe.wait_ge((x1_ready, x2_ready)[layer], t)
                w, rows = (w0_sb, w1_sb, w2_sb)[layer], ROWS0 if layer == 0 else P
                for g in range(GROUPS[layer]):
                    if is_split(layer, g):
                        part = SPLIT.index(g) % PARTS
                        for c in chunks_of(layer, g):
                            k, n = c % WIDTH, SPLIT_CHUNKS.index(c)
                            if k == 0:
                                pe.wait_ge(hi_made, look_up("split", i, j, layer, g) + 1)
                            nc.tensor.matmul(z[layer][:], w_lo[:, layer - 1, n, :], hi[:, part, k, :],
                                             start=False, stop=False)
                            nc.tensor.matmul(z[layer][:], w_hi[:, layer - 1, n, :], hi[:, part, k, :],
                                             start=False, stop=False)
                            if k == 0:
                                pe.wait_ge(lo_made, look_up("split", i, j, layer, g) + 1)
                            mm = nc.tensor.matmul(z[layer][:], w_hi[:, layer - 1, n, :], lo[:, part, k, :],
                                                  start=False, stop=False)
                    else:
                        pe.wait_ge(group_made, look_up("number", i, j, layer, g) + 1)
                        for c in chunks_of(layer, g):
                            n = c if layer == 0 else WHOLE_CHUNKS.index(c)
                            mm = nc.tensor.matmul(z[layer][:], w[0:rows, n, :],
                                                  prod[0:rows, slot_of(layer, g), c % WIDTH, :], start=(c == 0),
                                                  stop=(c == chunks_of(layer, GROUPS[layer] - 1)[-1]))
                    mm.then_inc(group_used, 1)

            def top1(b):
                pe.wait_ge(pooled_ready, 2 * (b + 1))
                for m in range(TOP1 // P):
                    for k in range(2):
                        nc.tensor.matmul(h1_ps[:, m, :], wt1_sb[:, k, m * P:(m + 1) * P], pooled[:, k, :],
                                         start=(k == 0), stop=False)
                    mm = nc.tensor.matmul(h1_ps[:, m, :], wt1d_sb[:, m * P:(m + 1) * P],
                                          dense_sb[:, bass.ds(b * BT, BT)], start=False, stop=True)
                mm.then_inc(h1_done, 1)

            def top2(b):
                pe.wait_ge(h1_ready, 4 * (b + 1))
                for m in range(TOP2 // P):
                    for k in range(TOP1 // P):
                        mm = nc.tensor.matmul(h2_ps[:, m, :], wt2_sb[:, k, m * P:(m + 1) * P], h1[:, k, :],
                                              start=(k == 0), stop=(k == TOP1 // P - 1))
                mm.then_inc(h2_done, 1)

            def top3(b):
                pe.wait_ge(h2_ready, 2 * (b + 1))
                for k in range(TOP2 // P):
                    mm = nc.tensor.matmul(y_ps[:, 0:BT], wt3_sb[:, k:k + 1], h2[:, k, :],
                                          start=(k == 0), stop=(k == TOP2 // P - 1))
                mm.then_inc(y_done, 1)

            def step(i, j):
                top = (not known(i) or i > 0)
                if tile_exists(i, j, 0):
                    interact(i, j, 0)
                if tile_exists(i, j, -2):
                    turn_tile(i, j, -2)
                if top and j == 3:
                    top2(i - 1)
                if tile_exists(i, j, 1):
                    interact(i, j, 1)
                if top and j == 3:
                    top3(i - 1)
                if top and j == 2:
                    top1(i - 1)
                if tile_exists(i, j, 2):
                    interact(i, j, 2)

            pe.wait_ge(id_landed, 16)
            turn_tile(0, 0, 0)
            turn_tile(0, 1, 0)
            pe.wait_ge(w0_summed, 1)
            pe.wait_ge(lo_weights, 1)
            pe.wait_ge(w_landed, 32)
            pe.wait_ge(top_landed, 80)
            for j in range(TPB):
                step(0, j)
            with pe.Fori(1, NBT - 1) as i:
                for j in range(TPB):
                    step(i, j)
            for j in range(TPB + 2):
                if j < TPB:
                    step(NBT - 1, j)
                elif j == TPB:
                    interact(NBT - 1, j, 1)
                    interact(NBT - 1, j, 2)
                else:
                    interact(NBT - 1, j, 2)
            top1(NBT - 1)
            top2(NBT - 1)
            top3(NBT - 1)

        @block.vector
        def _(dve):
            def lo_part(i, j, layer, g):
                part = SPLIT.index(g) % PARTS
                dve.wait_ge(hi_made, look_up("split", i, j, layer, g) + 1)
                nc.vector.tensor_tensor(lo[:, part], prod[:, slot_of(layer, g)], hi[:, part],
                                        ALU.subtract).then_inc(lo_made, 1)

            def products(i, j, layer):
                lag = layer
                if layer == 0:
                    dve.wait_ge(rot_landed, 16 * REP0 * (TPB * i + j + 1))
                else:
                    dve.wait_ge(spreads_landed[layer - 1], 32 * (TPB * i + j - lag + 1))
                for g in range(GROUPS[layer]):
                    whole, split = look_up("whole_held", i, j, layer, g), look_up("split_held", i, j, layer, g)
                    if whole is not None:
                        dve.wait_ge(group_used, whole + 1)
                    if split is not None:
                        dve.wait_ge(lo_made, split + 1)
                    c0, n = chunks_of(layer, g)[0], len(chunks_of(layer, g))
                    if layer == 0:
                        rows = ROWS0
                        left, right = x0[:, j % X0_SLOTS:j % X0_SLOTS + 1, :], x0_rot[:, c0:c0 + n, :]
                    else:
                        rows = P
                        left = x0_spread[layer - 1][:, c0 // NJ:c0 // NJ + 1, :]
                        right = x_spread[layer - 1][:, c0 % NJ:c0 % NJ + n, :]
                    nc.vector.tensor_tensor(prod[0:rows, slot_of(layer, g), 0:n, :],
                                            left.to_broadcast([rows, n, COLS]), right,
                                            ALU.mult).then_inc(group_made, 1)
                    if is_split(layer, g - LO_LAG):
                        lo_part(i, j, layer, g - LO_LAG)
                    if layer == 2 and g == 1:
                        sums(i, j)
                for g in range(GROUPS[layer] - LO_LAG, GROUPS[layer]):
                    if is_split(layer, g):
                        lo_part(i, j, layer, g)

            def sum_direct(i, j):
                t = TPB * i + j - 2
                dve.wait_ge(direct_ready[0], t + 1)
                dve.wait_ge(direct_ready[1], t + 1)
                nc.vector.tensor_reduce(part[:, 0, :, (j - 2) % TPB],
                                        direct[:, (j - 2) % 4, :].rearrange("p (d b) -> p b d", d=DT),
                                        AX.X, ALU.add).then_inc(direct_summed, 1)

            def sum_direct2(i, j):
                t = TPB * i + j - 3
                dve.wait_ge(direct_ready[2], t + 1)
                nc.vector.tensor_reduce(part[:, 1, :, (j - 3) % TPB],
                                        direct2[:, (j - 3) % 2, :].rearrange("p (d b) -> p b d", d=DT),
                                        AX.X, ALU.add).then_inc(direct2_summed, 1)

            def pool_batch_tile(b, layer01):
                if layer01:
                    dve.wait_ge(direct_summed, TPB * (b + 1))
                else:
                    dve.wait_ge(direct2_summed, TPB * (b + 1))
                k = 0 if layer01 else 1
                nc.vector.tensor_reduce(pooled[:, k, :], part[:, k, :, :],
                                        AX.X, ALU.add).then_inc(pooled_ready, 1)

            def sums(i, j):
                top = not known(i) or i > 0
                if tile_exists(i, j, 2):
                    sum_direct(i, j)
                    if j == 1 and top:
                        pool_batch_tile(i - 1, True)
                if tile_exists(i, j, 3):
                    sum_direct2(i, j)
                    if j == 2 and top:
                        pool_batch_tile(i - 1, False)

            def step(i, j):
                for layer in range(3):
                    if tile_exists(i, j, layer):
                        products(i, j, layer)

            dve.wait_ge(w0_landed, 32)
            nc.vector.tensor_tensor(w0_sb[:], w0_sb[:], w0b_sb, ALU.add).then_inc(w0_summed, 1)
            dve.wait_ge(hi_weights, 1)
            nc.vector.tensor_tensor(w_lo[:], stage, w_hi[:], ALU.subtract).then_inc(lo_weights, 1)
            dve.wait_ge(lo_weights, 1)
            for j in range(TPB):
                step(0, j)
            with dve.Fori(1, NBT - 1) as i:
                for j in range(TPB):
                    step(i, j)
            for j in range(TPB):
                step(NBT - 1, j)
            last = NBT - 1
            step(last, TPB)
            step(last, TPB + 1)
            pool_batch_tile(last, True)
            sum_direct2(last, TPB + 2)
            pool_batch_tile(last, False)

        @block.scalar
        def _(act):
            def hi_part(i, j, layer, g):
                held = look_up("part_held", i, j, layer, g)
                act.wait_ge(group_made, look_up("number", i, j, layer, g) + 1)
                if held is not None:
                    act.wait_ge(group_used, held + 1)
                nc.scalar.copy(hi[:, SPLIT.index(g) % PARTS], prod[:, slot_of(layer, g)]).then_inc(hi_made, 1)

            def leave(i, j, layer):
                t, jt = TPB * i + j - layer, j - layer
                act.wait_ge(group_used, look_up("number", i, j, layer) + GROUPS[layer])
                zl, b = z[layer], bias_sb[:, layer:layer + 1]
                if layer == 2:
                    nc.scalar.activation(direct2[:, jt % 2, :], zl[:], ACT.Relu,
                                         bias=b).then_inc(direct_ready[2], 1)
                    return
                on = slice(0, HALF) if layer == 0 else slice(HALF, P)
                stay = slice(HALF, P) if layer == 0 else slice(0, HALF)
                x, ready, saved = ((x1, x1_ready, x1_saved), (x2, x2_ready, x2_saved))[layer]
                if tile_exists(i, j, layer + 1):
                    act.wait_ge(saved, 16 * t)
                nc.scalar.activation(x[on, :], zl[on, :], ACT.Relu,
                                     bias=b[on, :]).then_inc(ready, 1)
                nc.scalar.activation(direct[stay, jt % 4, :], zl[stay, :], ACT.Relu,
                                     bias=b[stay, :]).then_inc(direct_ready[layer], 1)

            def order_rows(b):
                act.wait_ge(rows_gathered, 16 * FIELDS * (b + 1))
                if not known(b) or b > 0:
                    act.wait_ge(tile_turned, TPB * b)
                for r in range(REP0):
                    nc.scalar.copy(emb[:, :, r * FIELDS:(r + 1) * FIELDS],
                                   gathered[:].rearrange("p f d -> p d f")).then_inc(emb_ready, 1)

            def take_x0(i, j, lag):
                t = TPB * i + j - lag
                act.wait_ge(tile_turned, t + 1)
                nc.scalar.copy(x0[:, (j - lag) % X0_SLOTS, :],
                               turned[0:ROWS0, (j - lag) % 2, :]).then_inc(x0_ready, 1)

            def relu_top(b, src, dst, chunks, done, ready, col):
                act.wait_ge(done, b + 1)
                for m in range(chunks):
                    nc.scalar.activation(dst[:, m, :], src[:, m, :], ACT.Relu,
                                         bias=bias_sb[:, col + m:col + m + 1]).then_inc(ready, 1)

            def relu_top1(b):
                relu_top(b, h1_ps, h1, TOP1 // P, h1_done, h1_ready, 3)

            def relu_top2(b):
                relu_top(b, h2_ps, h2, TOP2 // P, h2_done, h2_ready, 3 + TOP1 // P)

            def take_y(b):
                act.wait_ge(y_done, b + 1)
                nc.scalar.copy(y[:, bass.ds(b * BT, BT)], y_ps[:, 0:BT]).then_inc(y_ready, 1)

            def step(i, j):
                top = not known(i) or i > 0
                for layer in range(3):
                    for g in range(GROUPS[layer]):
                        if is_split(layer, g) and tile_exists(i, j, layer):
                            hi_part(i, j, layer, g)
                        place = PLACE0[layer] + g
                        if place == LEAVE:
                            if tile_exists(i, j, 3):
                                leave(i, j - 1, 2)
                        if place == PLACE0[1] + LEAVE:
                            if tile_exists(i, j, 0):
                                leave(i, j, 0)
                            if tile_exists(i, j, -2):
                                take_x0(i, j, -2)
                            if j == 1 and (not known(i) or i < NBT - 1):
                                order_rows(i + 1)
                            if top and j == 3:
                                relu_top2(i - 1)
                        if place == PLACE0[2] + LEAVE:
                            if tile_exists(i, j, 1):
                                leave(i, j, 1)
                            if top and j == 2:
                                relu_top1(i - 1)
                            if top and j == 3:
                                take_y(i - 1)

            act.wait_ge(stage_landed, 32)
            nc.scalar.copy(w_hi[:], stage).then_inc(hi_weights, 1)
            act.wait_ge(bias_landed, 16)
            order_rows(0)
            take_x0(0, 0, 0)
            take_x0(0, 1, 0)
            for j in range(TPB):
                step(0, j)
            with act.Fori(1, NBT - 1) as i:
                for j in range(TPB):
                    step(i, j)
            last = NBT - 1
            for j in range(TPB):
                step(last, j)
            step(last, TPB)
            step(last, TPB + 1)
            leave(last, TPB + 1, 2)
            relu_top1(last)
            relu_top2(last)
            take_y(last)


def kernel(**inputs):
    import numpy as np
    import concourse.bacc as bacc
    from concourse.bass_utils import run_bass_kernel_spmd

    given = {k: np.asarray(v) for k, v in inputs.items()}

    w0 = given["L0_rec_w0"]
    w0a = np.zeros((ROWS0, CH0, SIZE), w0.dtype)
    w0b = np.zeros((ROWS0, CH0, SIZE), w0.dtype)
    h = np.arange(FIELDS)
    for delta in range(DELTAS):
        rows, c = slice(delta % REP0 * FIELDS, (delta % REP0 + 1) * FIELDS), delta // REP0
        w0a[rows, c] = w0[h, (h + delta) % FIELDS]
        if delta:
            w0b[rows, c] = w0[(h + delta) % FIELDS, h]

    def spread_weights(w):
        padded = np.zeros((R * NI, HALF, SIZE), w.dtype)
        padded[:FIELDS] = w
        return padded.reshape(R, NI, C, NJ, SIZE).transpose(2, 0, 1, 3, 4).reshape(P, CHK, SIZE)

    def swap(w, axis):
        return np.concatenate([w.take(range(HALF, SIZE), axis), w.take(range(HALF), axis)], axis)

    def columns(v):
        return v.reshape(-1, P).T

    t1 = given["W_top1"]
    w1 = spread_weights(swap(given["L0_rec_w1"], 2))
    w2 = spread_weights(given["L0_rec_w2"])
    arrays = {
        "ids": given["ids"].reshape(NBT, BT, FIELDS),
        "ident": np.eye(P, dtype=np.float32),
        "w0a": w0a,
        "w0b": w0b,
        "w1": w1[:, WHOLE_CHUNKS],
        "w2": w2[:, WHOLE_CHUNKS],
        "w1s": w1[:, SPLIT_CHUNKS],
        "w2s": w2[:, SPLIT_CHUNKS],
        "biases": np.concatenate([columns(v) for v in (given["L0_rec_b0"], swap(given["L0_rec_b1"], 0),
                                                       given["L0_rec_b2"], given["b_top1"], given["b_top2"])], 1),
        "dense_t": given["dense_ctx"].T,
        "wt1": np.stack([np.concatenate([t1[HALF:2 * HALF], t1[:HALF]]), t1[P:2 * P]], 1),
        "wt1d": t1[2 * P:],
        "wt2": given["W_top2"].reshape(TOP1 // P, P, TOP2).transpose(1, 0, 2),
        "wt3": given["W_top3"].reshape(TOP2 // P, P).T,
    }
    for f in range(FIELDS):
        arrays[f"tbl_{f}"] = given[f"tbl_{f}"]
    arrays = {k: np.ascontiguousarray(v) for k, v in arrays.items()}

    nc = bacc.Bacc("TRN2", target_bir_lowering=False, num_devices=1)
    aps = {k: nc.dram_tensor(k, v.shape, mybir.dt.from_np(v.dtype), kind="ExternalInput").ap()
           for k, v in arrays.items()}
    out = nc.dram_tensor("out", (BATCH, 1), F32, kind="ExternalOutput").ap()
    tables = [aps.pop(f"tbl_{f}") for f in range(FIELDS)]
    build(nc, tables, out=out, **aps)
    r = run_bass_kernel_spmd(nc, [arrays], core_ids=[0])
    return r.results[0]["out"]
```
